# Optimizing a Trainium2 kernel written in Bass

```python
import numpy as np
import jax
import jax.numpy as jnp

def _softmax(x, axis=-1):
    return jax.nn.softmax(x, axis=axis)

def _gelu(x):
    return jax.nn.gelu(x, approximate=True)

def _silu(x):
    return jax.nn.silu(x)

def _sigmoid(x):
    return jax.nn.sigmoid(x)

def _layernorm(x, axis=-1, eps=1e-05):
    m = jnp.mean(x, axis=axis, keepdims=True)
    v = jnp.var(x, axis=axis, keepdims=True)
    return (x - m) / jnp.sqrt(v + eps)

def _scatter_add(tgt, idx, src, axis=0):
    return tgt.at[idx].add(src)

def _segment_sum(src, seg, n):
    return jax.ops.segment_sum(src, seg, n)
kernel_name = 'mk_dlrm_tower_d1_rec_r8_b9d384'

def setup_inputs(seed: int=0):
    np.random.seed(seed)
    _w = jnp.asarray

    def _rec_inputs():
        import jax
        import jax.numpy as jnp
        _tk = jax.random.key(seed)
        dense_ctx = jax.random.normal(jax.random.fold_in(_tk, 190), (2048, 16), jnp.float32)
        ids = jnp.stack([jax.random.randint(jax.random.fold_in(_tk, 200 + f), (2048,), 0, v, jnp.int32) for f, v in enumerate([1250, 12500, 1000, 1250, 1000, 1000, 1000, 1250, 1000, 1000, 1250, 1250, 12500, 12500, 1000, 12500, 12500, 1250, 1000, 12500, 1250, 12500, 12500, 1250, 1000, 1250, 1000, 1000, 1250, 1000, 1000, 1250])], axis=1)
        tbl_0 = 0.05 * jax.random.normal(jax.random.fold_in(_tk, 500 + 0), (1250, 256), jnp.float32)
        tbl_1 = 0.05 * jax.random.normal(jax.random.fold_in(_tk, 500 + 1), (12500, 256), jnp.float32)
        tbl_2 = 0.05 * jax.random.normal(jax.random.fold_in(_tk, 500 + 2), (1000, 256), jnp.float32)
        tbl_3 = 0.05 * jax.random.normal(jax.random.fold_in(_tk, 500 + 3), (1250, 256), jnp.float32)
        tbl_4 = 0.05 * jax.random.normal(jax.random.fold_in(_tk, 500 + 4), (1000, 256), jnp.float32)
        tbl_5 = 0.05 * jax.random.normal(jax.random.fold_in(_tk, 500 + 5), (1000, 256), jnp.float32)
        tbl_6 = 0.05 * jax.random.normal(jax.random.fold_in(_tk, 500 + 6), (1000, 256), jnp.float32)
        tbl_7 = 0.05 * jax.random.normal(jax.random.fold_in(_tk, 500 + 7), (1250, 256), jnp.float32)
        tbl_8 = 0.05 * jax.random.normal(jax.random.fold_in(_tk, 500 + 8), (1000, 256), jnp.float32)
        tbl_9 = 0.05 * jax.random.normal(jax.random.fold_in(_tk, 500 + 9), (1000, 256), jnp.float32)
        tbl_10 = 0.05 * jax.random.normal(jax.random.fold_in(_tk, 500 + 10), (1250, 256), jnp.float32)
        tbl_11 = 0.05 * jax.random.normal(jax.random.fold_in(_tk, 500 + 11), (1250, 256), jnp.float32)
        tbl_12 = 0.05 * jax.random.normal(jax.random.fold_in(_tk, 500 + 12), (12500, 256), jnp.float32)
        tbl_13 = 0.05 * jax.random.normal(jax.random.fold_in(_tk, 500 + 13), (12500, 256), jnp.float32)
        tbl_14 = 0.05 * jax.random.normal(jax.random.fold_in(_tk, 500 + 14), (1000, 256), jnp.float32)
        tbl_15 = 0.05 * jax.random.normal(jax.random.fold_in(_tk, 500 + 15), (12500, 256), jnp.float32)
        tbl_16 = 0.05 * jax.random.normal(jax.random.fold_in(_tk, 500 + 16), (12500, 256), jnp.float32)
        tbl_17 = 0.05 * jax.random.normal(jax.random.fold_in(_tk, 500 + 17), (1250, 256), jnp.float32)
        tbl_18 = 0.05 * jax.random.normal(jax.random.fold_in(_tk, 500 + 18), (1000, 256), jnp.float32)
        tbl_19 = 0.05 * jax.random.normal(jax.random.fold_in(_tk, 500 + 19), (12500, 256), jnp.float32)
        tbl_20 = 0.05 * jax.random.normal(jax.random.fold_in(_tk, 500 + 20), (1250, 256), jnp.float32)
        tbl_21 = 0.05 * jax.random.normal(jax.random.fold_in(_tk, 500 + 21), (12500, 256), jnp.float32)
        tbl_22 = 0.05 * jax.random.normal(jax.random.fold_in(_tk, 500 + 22), (12500, 256), jnp.float32)
        tbl_23 = 0.05 * jax.random.normal(jax.random.fold_in(_tk, 500 + 23), (1250, 256), jnp.float32)
        tbl_24 = 0.05 * jax.random.normal(jax.random.fold_in(_tk, 500 + 24), (1000, 256), jnp.float32)
        tbl_25 = 0.05 * jax.random.normal(jax.random.fold_in(_tk, 500 + 25), (1250, 256), jnp.float32)
        tbl_26 = 0.05 * jax.random.normal(jax.random.fold_in(_tk, 500 + 26), (1000, 256), jnp.float32)
        tbl_27 = 0.05 * jax.random.normal(jax.random.fold_in(_tk, 500 + 27), (1000, 256), jnp.float32)
        tbl_28 = 0.05 * jax.random.normal(jax.random.fold_in(_tk, 500 + 28), (1250, 256), jnp.float32)
        tbl_29 = 0.05 * jax.random.normal(jax.random.fold_in(_tk, 500 + 29), (1000, 256), jnp.float32)
        tbl_30 = 0.05 * jax.random.normal(jax.random.fold_in(_tk, 500 + 30), (1000, 256), jnp.float32)
        tbl_31 = 0.05 * jax.random.normal(jax.random.fold_in(_tk, 500 + 31), (1250, 256), jnp.float32)
        _rk = jax.random.fold_in(_tk, 7)
        W_top1 = 0.0441942 * jax.random.normal(jax.random.fold_in(_tk, 801), (512, 512), jnp.float32)
        W_top2 = 0.0441942 * jax.random.normal(jax.random.fold_in(_tk, 802), (512, 256), jnp.float32)
        W_top3 = 0.0625 * jax.random.normal(jax.random.fold_in(_tk, 803), (256, 1), jnp.float32)
        b_top1 = jnp.zeros((512,), jnp.float32)
        b_top2 = jnp.zeros((256,), jnp.float32)
        return (dense_ctx, ids, tbl_0, tbl_1, tbl_2, tbl_3, tbl_4, tbl_5, tbl_6, tbl_7, tbl_8, tbl_9, tbl_10, tbl_11, tbl_12, tbl_13, tbl_14, tbl_15, tbl_16, tbl_17, tbl_18, tbl_19, tbl_20, tbl_21, tbl_22, tbl_23, tbl_24, tbl_25, tbl_26, tbl_27, tbl_28, tbl_29, tbl_30, tbl_31, W_top1, b_top1, W_top2, b_top2, W_top3)
    dense_ctx, ids, tbl_0, tbl_1, tbl_2, tbl_3, tbl_4, tbl_5, tbl_6, tbl_7, tbl_8, tbl_9, tbl_10, tbl_11, tbl_12, tbl_13, tbl_14, tbl_15, tbl_16, tbl_17, tbl_18, tbl_19, tbl_20, tbl_21, tbl_22, tbl_23, tbl_24, tbl_25, tbl_26, tbl_27, tbl_28, tbl_29, tbl_30, tbl_31, W_top1, b_top1, W_top2, b_top2, W_top3 = _rec_inputs()

    def _L0_rec_setup():
        import jax, jax.numpy as jnp
        import numpy as np
        B, N, D = (1024, 32, 256)
        key = jax.random.key(seed)
        x = jax.random.normal(key, (B, N, D), dtype=jnp.float32)
        return {'x': x}
    _L0_rec_all = _L0_rec_setup()
    _L0_rec_in = {k: v for k, v in _L0_rec_all.items() if k in ()}
    del _L0_rec_all
    return {'dense_ctx': dense_ctx, 'ids': ids, 'tbl_0': tbl_0, 'tbl_1': tbl_1, 'tbl_2': tbl_2, 'tbl_3': tbl_3, 'tbl_4': tbl_4, 'tbl_5': tbl_5, 'tbl_6': tbl_6, 'tbl_7': tbl_7, 'tbl_8': tbl_8, 'tbl_9': tbl_9, 'tbl_10': tbl_10, 'tbl_11': tbl_11, 'tbl_12': tbl_12, 'tbl_13': tbl_13, 'tbl_14': tbl_14, 'tbl_15': tbl_15, 'tbl_16': tbl_16, 'tbl_17': tbl_17, 'tbl_18': tbl_18, 'tbl_19': tbl_19, 'tbl_20': tbl_20, 'tbl_21': tbl_21, 'tbl_22': tbl_22, 'tbl_23': tbl_23, 'tbl_24': tbl_24, 'tbl_25': tbl_25, 'tbl_26': tbl_26, 'tbl_27': tbl_27, 'tbl_28': tbl_28, 'tbl_29': tbl_29, 'tbl_30': tbl_30, 'tbl_31': tbl_31, 'W_top1': W_top1, 'b_top1': b_top1, 'W_top2': W_top2, 'b_top2': b_top2, 'W_top3': W_top3}

def reference(dense_ctx, ids, tbl_0, tbl_1, tbl_2, tbl_3, tbl_4, tbl_5, tbl_6, tbl_7, tbl_8, tbl_9, tbl_10, tbl_11, tbl_12, tbl_13, tbl_14, tbl_15, tbl_16, tbl_17, tbl_18, tbl_19, tbl_20, tbl_21, tbl_22, tbl_23, tbl_24, tbl_25, tbl_26, tbl_27, tbl_28, tbl_29, tbl_30, tbl_31, W_top1, b_top1, W_top2, b_top2, W_top3):
    import jax
    import jax.numpy as jnp

    def _L0_rec_ref(x):
        import jax, jax.numpy as jnp
        import numpy as np
        B, N, D = (1024, 32, 256)
        'Second-order feature interaction (DLRM dot interaction).\n\n            Computes dot(x_i, x_j) for all field pairs i < j (self_interaction=False),\n            flattened in row-major upper-triangular order -> [B, N*(N-1)/2].\n            Matches tf.boolean_mask(dot_products, strictly_upper_mask) ordering.\n            '
        b, n, d = x.shape
        iu, ju = jnp.triu_indices(n, k=1)
        dots = jnp.einsum('bnd,bmd->bnm', x, x)
        return dots[:, iu, ju]
    e = jnp.stack([tbl_0[ids[:, 0]], tbl_1[ids[:, 1]], tbl_2[ids[:, 2]], tbl_3[ids[:, 3]], tbl_4[ids[:, 4]], tbl_5[ids[:, 5]], tbl_6[ids[:, 6]], tbl_7[ids[:, 7]], tbl_8[ids[:, 8]], tbl_9[ids[:, 9]], tbl_10[ids[:, 10]], tbl_11[ids[:, 11]], tbl_12[ids[:, 12]], tbl_13[ids[:, 13]], tbl_14[ids[:, 14]], tbl_15[ids[:, 15]], tbl_16[ids[:, 16]], tbl_17[ids[:, 17]], tbl_18[ids[:, 18]], tbl_19[ids[:, 19]], tbl_20[ids[:, 20]], tbl_21[ids[:, 21]], tbl_22[ids[:, 22]], tbl_23[ids[:, 23]], tbl_24[ids[:, 24]], tbl_25[ids[:, 25]], tbl_26[ids[:, 26]], tbl_27[ids[:, 27]], tbl_28[ids[:, 28]], tbl_29[ids[:, 29]], tbl_30[ids[:, 30]], tbl_31[ids[:, 31]]], axis=1)
    z = _L0_rec_ref(e)
    z = z.reshape(z.shape[0], -1)
    h = jnp.concatenate([z, dense_ctx], axis=1)
    h = jnp.maximum(h @ W_top1 + b_top1, 0.0)
    h = jnp.maximum(h @ W_top2 + b_top2, 0.0)
    y = h @ W_top3
    return y

_drawn_inputs = setup_inputs


def setup_inputs(seed=0):
    import zlib

    import numpy as np

    out = dict(_drawn_inputs(seed))
    spreads = {'b_top1': (0.0, 0.1), 'b_top2': (0.0, 0.1)}
    factors = {}
    for name, (base, spread) in spreads.items():
        noise = np.random.default_rng([zlib.crc32(name.encode()), seed]).standard_normal(out[name].shape)
        drawn = base * np.exp(spread * noise) if base else spread * noise
        out[name] = jnp.asarray(drawn.astype(out[name].dtype))
    for name, factor in factors.items():
        out[name] = (out[name] * factor).astype(out[name].dtype)
    return out
```

```python
from contextlib import ExitStack

import numpy as np

import concourse.bass as bass
import concourse.mybir as mybir

FIELDS = 32
D = 256
P = 128
BATCH = 2048
CONTEXT = 16
HALF = FIELDS // 2
PAIRS = FIELDS * (FIELDS - 1) // 2
CYCLIC = FIELDS * (HALF - 1)
HIDDEN1 = 512
HIDDEN2 = 256


def pair_order():
    upper = np.zeros((FIELDS, FIELDS), np.int64)
    rows, cols = np.triu_indices(FIELDS, k=1)
    upper[rows, cols] = upper[cols, rows] = np.arange(PAIRS)
    order = [upper[i, (i + k) % FIELDS] for i in range(FIELDS) for k in range(1, HALF)]
    order += [upper[i, i + HALF] for i in range(HALF)]
    order += list(range(PAIRS, PAIRS + CONTEXT))
    return np.array(order)


def dlrm_tower(nc, dense_ctx, ids, tables, w1, b1, w2, b2, w3, out):
    fp32 = mybir.dt.float32
    int32 = mybir.dt.int32
    ALU = mybir.AluOpType
    ACT = mybir.ActivationFunctionType

    TILES = BATCH // P
    CHUNKS = D // P
    TURNED = 4
    STEPS = FIELDS // TURNED
    COLS = 4
    GROUPS = P // COLS
    GPS = GROUPS // STEPS
    FEATURES = PAIRS + CONTEXT
    KC = FEATURES // P
    M1 = HIDDEN1 // P
    M2 = HIDDEN2 // P
    ZROW = FIELDS + HALF

    ctx = ExitStack()
    with ctx:
        def sbuf(name, shape, dt=fp32):
            return ctx.enter_context(nc.sbuf_tensor(name, shape, dt))

        def psum(name, shape):
            return ctx.enter_context(nc.psum_tensor(name, shape, fp32))

        def sem(name):
            return ctx.enter_context(nc.semaphore(name))

        row_ids = [sbuf(f"row_ids{i}", [P, FIELDS], int32) for i in range(2)]
        rows = sbuf("rows", [P, FIELDS, D])
        turned = [sbuf(f"turned{i}", [P, CHUNKS, FIELDS, P]) for i in range(2)]
        products = sbuf("products", [P, FIELDS * (ZROW + 1)])
        features = [sbuf(f"features{i}", [P, FEATURES]) for i in range(2)]
        features_t = sbuf("features_t", [P, KC, P])
        hidden1 = sbuf("hidden1", [P, M1, P])
        hidden2 = sbuf("hidden2", [P, M2, P])
        y_row = sbuf("y_row", [1, BATCH])
        w1_sb = sbuf("w1_sb", [P, KC, HIDDEN1])
        w2_sb = sbuf("w2_sb", [P, M1, HIDDEN2])
        w3_sb = sbuf("w3_sb", [P, M2])
        b1_sb = sbuf("b1_sb", [P, M1])
        b2_sb = sbuf("b2_sb", [P, M2])
        ident = sbuf("ident", [P, P])

        turn_ps = [[psum(f"turn_ps{i}{c}", [P, TURNED * P]) for c in range(CHUNKS)] for i in range(2)]
        gram_ps = psum("gram_ps", [P, GROUPS * FIELDS])
        bank_a = psum("bank_a", [P, KC * P])
        bank_b = psum("bank_b", [P, M1 * P])

        ids_in = [sem(f"ids_in{i}") for i in range(2)]
        dense_in = [sem(f"dense_in{i}") for i in range(2)]
        weights_in = sem("weights_in")
        slots_open = sem("slots_open")
        gathered = [sem(f"gathered{k}") for k in range(STEPS)]
        ident_zero = sem("ident_zero")
        ident_ready = sem("ident_ready")
        step_turned = sem("step_turned")
        act_kept = sem("act_kept")
        dve_kept = sem("dve_kept")
        gram_done = sem("gram_done")
        gram_read = sem("gram_read")
        wrapped = sem("wrapped")
        picked = sem("picked")
        ft_done = sem("ft_done")
        ft_kept = sem("ft_kept")
        h1_done = sem("h1_done")
        h1_kept = sem("h1_kept")
        h2_done = sem("h2_done")
        h2_kept = sem("h2_kept")
        y_done = sem("y_done")
        y_kept = sem("y_kept")
        y_out = sem("y_out")

        block = ctx.enter_context(nc.Block())

        square = products[:, 0:FIELDS * ZROW].rearrange("p (i j) -> p i j", j=ZROW)
        diagonal = products[:, :].rearrange("p (i k) -> p i k", k=ZROW + 1)

        @block.sync
        def _(sp):
            def load_inputs(t, par, first):
                if not first:
                    sp.wait_ge(step_turned, (t - 1) * STEPS)
                sp.dma_start(row_ids[par][:, :], ids[bass.ds(t * P, P), :]).then_inc(ids_in[par], 16)
                if not first:
                    sp.wait_ge(ft_done, t - 1)
                sp.dma_start(features[par][:, PAIRS:FEATURES],
                             dense_ctx[bass.ds(t * P, P), :]).then_inc(dense_in[par], 16)

            load_inputs(0, 0, True)
            load_inputs(1, 1, True)
            sp.dma_start(w1_sb[:, :, :], w1.rearrange("(k p) n -> p k n", p=P)).then_inc(weights_in, 16)
            sp.dma_start(w2_sb[:, :, :], w2.rearrange("(k p) n -> p k n", p=P)).then_inc(weights_in, 16)
            sp.dma_start(w3_sb[:, :], w3).then_inc(weights_in, 16)
            sp.dma_start(b1_sb[:, :], b1).then_inc(weights_in, 16)
            sp.dma_start(b2_sb[:, :], b2).then_inc(weights_in, 16)
            with sp.Fori(1, TILES // 2) as u:
                for par in range(2):
                    load_inputs(u * 2 + par, par, False)
            sp.wait_ge(y_kept, TILES)
            sp.dma_start(out, y_row[:, :]).then_inc(y_out, 16)
            sp.wait_ge(y_out, 16)

        @block.gpsimd
        def _(pool):
            def gather(u, par, first):
                t = u * 2 + par
                pool.wait_ge(ids_in[par], (u + 1) * 16)
                pool.sem_inc(slots_open, 1)
                for f in range(FIELDS):
                    k = f // TURNED
                    if not first and f % TURNED == 0:
                        pool.wait_ge(step_turned, (t - 1) * STEPS + k + 1)
                        pool.sem_inc(slots_open, 1)
                    pool.indirect_dma_start(
                        out=rows[:, f, :], out_offset=None, in_=tables[f],
                        in_offset=bass.IndirectOffsetOnAxis(ap=row_ids[par][:, f:f + 1], axis=0),
                    ).then_inc(gathered[k], 16)

            pool.memset(ident[:, :], 0.0).then_inc(ident_zero, 1)
            pool.wait_ge(ident_zero, 1)
            pool.affine_select(out=ident[:, :], in_=ident[:, :], compare_op=ALU.not_equal, fill=1.0,
                               base=0, pattern=[[-1, P]], channel_multiplier=1).then_inc(ident_ready, 1)
            gather(0, 0, True)
            gather(0, 1, False)
            with pool.Fori(1, TILES // 2) as u:
                for par in range(2):
                    gather(u, par, False)

        @block.tensor
        def _(pe):
            def turn(t, k, first):
                pe.wait_ge(gathered[k], (t + 1) * 16 * TURNED)
                if not first:
                    pe.wait_ge(act_kept, t * STEPS + k - 1)
                    pe.wait_ge(dve_kept, t * STEPS + k - 1)
                for c in range(CHUNKS):
                    for j in range(TURNED):
                        last = pe.transpose(turn_ps[k % 2][c][:, j * P:(j + 1) * P],
                                            rows[:, k * TURNED + j, c * P:(c + 1) * P], ident[:, :])
                last.then_inc(step_turned, 1)

            def gram(t, par, k, first):
                if k == 0:
                    pe.wait_ge(act_kept, (t + 1) * STEPS)
                    pe.wait_ge(dve_kept, (t + 1) * STEPS)
                    if not first:
                        pe.wait_ge(gram_read, t)
                for g in range(k * GPS, (k + 1) * GPS):
                    for c in range(CHUNKS):
                        for q in range(COLS):
                            fields = turned[par][:, c, :, q * GROUPS + g]
                            last = pe.matmul(gram_ps[q * FIELDS:(q + 1) * FIELDS, g * FIELDS:(g + 1) * FIELDS],
                                             fields, fields, start=(c == 0), stop=(c == CHUNKS - 1))
                if k == STEPS - 1:
                    last.then_inc(gram_done, 1)

            def turn_features(u, par, first):
                t = u * 2 + par
                pe.wait_ge(picked, (t + 1) * 2)
                pe.wait_ge(dense_in[par], (u + 1) * 16)
                if not first:
                    pe.wait_ge(y_kept, t)
                for c in range(KC):
                    last = pe.transpose(bank_a[:, c * P:(c + 1) * P],
                                        features[par][:, c * P:(c + 1) * P], ident[:, :])
                last.then_inc(ft_done, 1)

            def layer1(t, ms):
                if ms[0] == 0:
                    pe.wait_ge(ft_kept, t + 1)
                for m in ms:
                    for c in range(KC):
                        last = pe.matmul(bank_b[:, m * P:(m + 1) * P], w1_sb[:, c, m * P:(m + 1) * P],
                                         features_t[:, c, :], start=(c == 0), stop=(c == KC - 1))
                if ms[-1] == M1 - 1:
                    last.then_inc(h1_done, 1)

            def layer2(t):
                pe.wait_ge(h1_kept, (t + 1) * M1)
                for m in range(M2):
                    for c in range(M1):
                        last = pe.matmul(bank_a[:, m * P:(m + 1) * P], w2_sb[:, c, m * P:(m + 1) * P],
                                         hidden1[:, c, :], start=(c == 0), stop=(c == M1 - 1))
                last.then_inc(h2_done, 1)

            def layer3(t):
                pe.wait_ge(h2_kept, (t + 1) * M2)
                for c in range(M2):
                    last = pe.matmul(bank_a[0:1, M2 * P:(M2 + 1) * P], w3_sb[:, c:c + 1],
                                     hidden2[:, c, :], start=(c == 0), stop=(c == M2 - 1))
                last.then_inc(y_done, 1)

            def mlp_part(u, par, k, first):
                t = u * 2 + par
                if k == 2:
                    turn_features(u, par, first)
                if k == 3:
                    layer1(t, range(0, M1 // 2))
                if k == 4:
                    layer1(t, range(M1 // 2, M1))
                if k == 5:
                    layer2(t)
                if k == 6:
                    layer3(t)

            pe.wait_ge(ident_ready, 1)
            for k in range(STEPS):
                turn(0, k, k < 2)
            for k in range(STEPS):
                turn(1, k, False)
                gram(0, 0, k, True)
            pe.wait_ge(weights_in, 16 * 5)
            for par in range(2):
                for k in range(STEPS):
                    turn(2 + par, k, False)
                    gram(1 + par, 1 - par, k, False)
                    mlp_part(0, par, k, par == 0)
            with pe.Fori(2, TILES // 2) as u:
                for par in range(2):
                    for k in range(STEPS):
                        turn(u * 2 + par, k, False)
                        gram(u * 2 + par - 1, 1 - par, k, False)
                        mlp_part(u - 1, par, k, False)
            last_pair = TILES // 2 - 1
            for k in range(STEPS):
                gram(TILES - 1, 1, k, False)
                mlp_part(last_pair, 0, k, False)
            for k in range(STEPS):
                mlp_part(last_pair, 1, k, False)

        @block.scalar
        def _(act):
            def keep_turned(t, par, k, first):
                act.wait_ge(step_turned, t * STEPS + k + 1)
                if k == 0 and not first:
                    act.wait_ge(gram_done, t - 1)
                act.activation(turned[par][:, 0, k * TURNED:(k + 1) * TURNED, :],
                               turn_ps[k % 2][0][:, :].rearrange("p (f s) -> p f s", f=TURNED),
                               ACT.Copy).then_inc(act_kept, 1)

            def pick(t, par, first):
                act.wait_ge(wrapped, t + 1)
                if not first:
                    act.wait_ge(ft_done, t - 1)
                act.activation(features[par][:, 0:CYCLIC].rearrange("p (i k) -> p i k", i=FIELDS),
                               diagonal[:, :, 1:HALF], ACT.Copy).then_inc(picked, 1)
                act.activation(features[par][:, CYCLIC:PAIRS], diagonal[:, 0:HALF, HALF],
                               ACT.Copy).then_inc(picked, 1)

            def keep_features(t):
                act.wait_ge(ft_done, t + 1)
                act.activation(features_t[:, :, :], bank_a[:, :].rearrange("p (k s) -> p k s", k=KC),
                               ACT.Copy).then_inc(ft_kept, 1)

            def keep_hidden1(t):
                act.wait_ge(h1_done, t + 1)
                for m in range(M1):
                    act.activation(hidden1[:, m, :], bank_b[:, m * P:(m + 1) * P], ACT.Relu,
                                   bias=b1_sb[:, m:m + 1]).then_inc(h1_kept, 1)

            def keep_hidden2(t):
                act.wait_ge(h2_done, t + 1)
                for m in range(M2):
                    act.activation(hidden2[:, m, :], bank_a[:, m * P:(m + 1) * P], ACT.Relu,
                                   bias=b2_sb[:, m:m + 1]).then_inc(h2_kept, 1)

            def keep_y(t):
                act.wait_ge(y_done, t + 1)
                act.activation(y_row[:, bass.ds(t * P, P)], bank_a[0:1, M2 * P:(M2 + 1) * P],
                               ACT.Copy).then_inc(y_kept, 1)

            def mlp_part(t, k):
                if k == 2:
                    keep_features(t)
                if k == 4:
                    keep_hidden1(t)
                if k == 5:
                    keep_hidden2(t)
                if k == 6:
                    keep_y(t)

            for k in range(STEPS):
                keep_turned(0, 0, k, True)
            for k in range(STEPS):
                keep_turned(1, 1, k, True)
            act.wait_ge(weights_in, 16 * 5)
            for par in range(2):
                for k in range(STEPS):
                    keep_turned(2 + par, par, k, False)
                    if k == 0:
                        pick(par, par, True)
                    mlp_part(par, k)
            with act.Fori(2, TILES // 2) as u:
                for par in range(2):
                    t = u * 2 + par
                    for k in range(STEPS):
                        keep_turned(t, par, k, False)
                        if k == 0:
                            pick(t - 2, par, False)
                        mlp_part(t - 2, k)
            for t in range(TILES - 2, TILES):
                pick(t, t % 2, False)
                for k in range(STEPS):
                    mlp_part(t, k)

        @block.vector
        def _(dve):
            def keep_turned(t, par, k, first):
                dve.wait_ge(step_turned, t * STEPS + k + 1)
                if k == 0 and not first:
                    dve.wait_ge(gram_done, t - 1)
                dve.tensor_copy(turned[par][:, 1, k * TURNED:(k + 1) * TURNED, :],
                                turn_ps[k % 2][1][:, :].rearrange("p (f s) -> p f s", f=TURNED),
                                ).then_inc(dve_kept, 1)

            def unfold(t, first):
                dve.wait_ge(gram_done, t + 1)
                if not first:
                    dve.wait_ge(picked, t * 2)
                dve.transpose(square[:, :, 0:FIELDS],
                              gram_ps[:, :].rearrange("p (g j) -> p j g", g=GROUPS)).then_inc(gram_read, 1)
                dve.wait_ge(gram_read, t + 1)
                dve.tensor_copy(square[:, :, FIELDS:ZROW], square[:, :, 0:HALF]).then_inc(wrapped, 1)

            for k in range(STEPS):
                keep_turned(0, 0, k, True)
            for k in range(STEPS):
                keep_turned(1, 1, k, True)
            for par in range(2):
                unfold(par, par == 0)
                for k in range(STEPS):
                    keep_turned(2 + par, par, k, False)
            with dve.Fori(2, TILES // 2) as u:
                for par in range(2):
                    t = u * 2 + par
                    unfold(t - 2, False)
                    for k in range(STEPS):
                        keep_turned(t, par, k, False)
            for t in range(TILES - 2, TILES):
                unfold(t, False)


def kernel(**inputs):
    import concourse.bacc as bacc
    from concourse.bass_utils import run_bass_kernel_spmd

    nc = bacc.Bacc("TRN2", target_bir_lowering=False, num_devices=1)
    laid = {name: np.ascontiguousarray(a) for name, a in inputs.items()}
    laid["W_top1"] = np.ascontiguousarray(laid["W_top1"][pair_order()])
    for name in ("b_top1", "b_top2", "W_top3"):
        laid[name] = np.ascontiguousarray(laid[name].reshape(-1, P).T)
    arrays, aps = {}, {}
    for name, a in laid.items():
        arrays[f"in_{name}"] = a
        aps[name] = nc.dram_tensor(f"in_{name}", a.shape, mybir.dt.from_np(a.dtype), kind="ExternalInput").ap()
    out = nc.dram_tensor("out_y", (1, BATCH), mybir.dt.float32, kind="ExternalOutput").ap()
    dlrm_tower(nc, aps["dense_ctx"], aps["ids"], [aps[f"tbl_{f}"] for f in range(FIELDS)],
               aps["W_top1"], aps["b_top1"], aps["W_top2"], aps["b_top2"], aps["W_top3"], out)
    r = run_bass_kernel_spmd(nc, [arrays], core_ids=[0])
    return r.results[0]["out_y"].reshape(BATCH, 1)
```

```python
from contextlib import ExitStack

import numpy as np

import concourse.bass as bass
import concourse.mybir as mybir

FIELDS = 32
D = 256
P = 128
BATCH = 2048
CONTEXT = 16
HALF = FIELDS // 2
PAIRS = FIELDS * (FIELDS - 1) // 2
CYCLIC = FIELDS * (HALF - 1)
HIDDEN1 = 512
HIDDEN2 = 256
SMALL_ROWS = 1000
SMALL_FIELDS = [2, 4]
SMALL = len(SMALL_FIELDS)
SLOTS = SMALL_FIELDS + [f for f in range(FIELDS) if f not in SMALL_FIELDS]


def pair_order():
    upper = np.zeros((FIELDS, FIELDS), np.int64)
    rows, cols = np.triu_indices(FIELDS, k=1)
    upper[rows, cols] = upper[cols, rows] = np.arange(PAIRS)
    upper = upper[np.ix_(SLOTS, SLOTS)]
    order = [upper[i, (i + k) % FIELDS] for i in range(FIELDS) for k in range(1, HALF)]
    order += [upper[i, i + HALF] for i in range(HALF)]
    order += list(range(PAIRS, PAIRS + CONTEXT))
    return np.array(order)


def dlrm_tower(nc, dense_ctx, ids, small_ids, tables, w1, b1, w2, b2, w3, out):
    fp32 = mybir.dt.float32
    fp32r = mybir.dt.float32r
    int32 = mybir.dt.int32
    ALU = mybir.AluOpType
    ACT = mybir.ActivationFunctionType

    TILES = BATCH // P
    CHUNKS = D // P
    TURNED = 4
    STEPS = FIELDS // TURNED
    QUADS = P // FIELDS
    GROUPS = P // QUADS
    PORTIONS = 8
    GPP = GROUPS // PORTIONS
    FEATURES = PAIRS + CONTEXT
    KC = FEATURES // P
    M1 = HIDDEN1 // P
    M2 = HIDDEN2 // P
    ZROW = FIELDS + HALF
    SUB = 8
    SP = SMALL_ROWS // SUB
    GATHERED0 = TURNED - SMALL
    LOADED = 5

    ctx = ExitStack()
    with ctx:
        def sbuf(name, shape, dt=fp32):
            return ctx.enter_context(nc.sbuf_tensor(name, shape, dt))

        def psum(name, shape):
            return ctx.enter_context(nc.psum_tensor(name, shape, fp32))

        def sem(name):
            return ctx.enter_context(nc.semaphore(name))

        row_ids = [sbuf(f"row_ids{i}", [P, FIELDS], int32) for i in range(2)]
        ids_across = sbuf("ids_across", [SP, SMALL, P], int32)
        sub_row = sbuf("sub_row", [SP, SUB], int32)
        one_hot = sbuf("one_hot", [SP, SUB, SMALL, P], fp32r)
        small = sbuf("small", [SP, SMALL, SUB, 2, D], fp32r)
        rows = sbuf("rows", [P, FIELDS, D])
        turned = [sbuf(f"turned{i}", [P, CHUNKS, P, FIELDS]) for i in range(2)]
        gram_sb = sbuf("gram_sb", [P, GROUPS, FIELDS])
        products = sbuf("products", [P, FIELDS * (ZROW + 1)])
        features = sbuf("features", [P, FEATURES])
        features_t = sbuf("features_t", [P, KC, P])
        hidden1 = sbuf("hidden1", [P, M1, P])
        hidden2 = features_t[:, 0:M2, :]
        y_sb = sbuf("y_sb", [1, P])
        w1_sb = sbuf("w1_sb", [P, KC, HIDDEN1])
        w2_sb = sbuf("w2_sb", [P, M1, HIDDEN2])
        w3_sb = sbuf("w3_sb", [P, M2])
        b1_sb = sbuf("b1_sb", [P, M1])
        b2_sb = sbuf("b2_sb", [P, M2])
        ident = sbuf("ident", [P, P])

        work_ps = [psum(f"work_ps{i}", [P, 2, 512]) for i in range(2)]
        gram_ps = [psum(f"gram_ps{i}", [P, GPP, P]) for i in range(2)]
        bank_a = psum("bank_a", [P, KC * P])
        bank_b = psum("bank_b", [P, M1 * P])

        row_ids_in = [sem(f"row_ids_in{i}") for i in range(2)]
        ids_across_in = sem("ids_across_in")
        dense_in = sem("dense_in")
        weights_in = sem("weights_in")
        small_in = sem("small_in")
        gathered = [sem(f"gathered{k}") for k in range(STEPS)]
        slots_open = sem("slots_open")
        ident_zero = sem("ident_zero")
        ident_ready = sem("ident_ready")
        sub_row_ready = sem("sub_row_ready")
        high_ready = sem("high_ready")
        low_ready = sem("low_ready")
        one_hot_made = sem("one_hot_made")
        produced = sem("produced")
        produced_kept = sem("produced_kept")
        step_turned = sem("step_turned")
        act_kept = sem("act_kept")
        dve_kept = sem("dve_kept")
        gram_done = sem("gram_done")
        act_cut = sem("act_cut")
        dve_cut = sem("dve_cut")
        unfolded = sem("unfolded")
        wrapped = sem("wrapped")
        picked = sem("picked")
        ft_done = sem("ft_done")
        ft_kept = sem("ft_kept")
        h1_done = sem("h1_done")
        h1_kept = sem("h1_kept")
        h2_done = sem("h2_done")
        h2_kept = sem("h2_kept")
        y_done = sem("y_done")
        y_kept = sem("y_kept")
        y_out = sem("y_out")

        block = ctx.enter_context(nc.Block())

        small_raw = turned[1][0:SP, :, :, :].rearrange("p c s f -> p (c s f)")[
            :, 0:SMALL * SUB * D].rearrange("p (t r d) -> p t r d", t=SMALL, r=SUB)
        square = products[:, 0:FIELDS * ZROW].rearrange("p (i j) -> p i j", j=ZROW)
        diagonal = products[:, :].rearrange("p (i k) -> p i k", k=ZROW + 1)
        quads = [t[:, :, :, :].rearrange("d c (g q) f -> d c g (q f)", q=QUADS) for t in turned]
        kept = [t[:, :, :, :].rearrange("d c (g q) f -> d c q g f", q=QUADS) for t in turned]

        def cut(engine_copy, portion):
            for q in range(QUADS):
                at = slice(q * FIELDS, (q + 1) * FIELDS)
                last = engine_copy(gram_sb[at, portion * GPP:(portion + 1) * GPP, :],
                                   gram_ps[portion % 2][at, :, at])
            return last

        @block.sync
        def _(sp):
            def load_row_ids(t, par):
                sp.dma_start(row_ids[par][:, :], ids[bass.ds(t * P, P), :]).then_inc(row_ids_in[par], 16)

            def load_ids_across(t):
                sp.dma_start(ids_across[:, :, :], small_ids[:, bass.ds(t * P, P)].partition_broadcast(SP),
                             ).then_inc(ids_across_in, 16)

            def load_dense(t):
                sp.dma_start(features[:, PAIRS:FEATURES],
                             dense_ctx[bass.ds(t * P, P), :]).then_inc(dense_in, 16)

            def store_y(t):
                sp.wait_ge(y_kept, t + 1)
                sp.dma_start(out[:, bass.ds(t * P, P)], y_sb[:, :]).then_inc(y_out, 16)

            def during(t, par):
                if not (isinstance(t, int) and t == TILES - 1):
                    sp.wait_ge(step_turned, t * STEPS)
                    load_row_ids(t + 1, 1 - par)
                if not (isinstance(t, int) and t >= TILES - 2):
                    sp.wait_ge(one_hot_made, t + 1)
                    load_ids_across(t + 2)
                if not (isinstance(t, int) and t < 2):
                    store_y(t - 2)
                sp.wait_ge(ft_done, t)
                load_dense(t)

            load_row_ids(0, 0)
            load_ids_across(1)
            for i in range(SMALL):
                sp.dma_start(small_raw[:, i, :, :], tables[i].rearrange("(p r) d -> p r d", r=SUB),
                             ).then_inc(small_in, 16)
            load_row_ids(1, 1)
            load_dense(0)
            sp.dma_start(w1_sb[:, :, :], w1.rearrange("(k p) n -> p k n", p=P)).then_inc(weights_in, 16)
            sp.dma_start(w2_sb[:, :, :], w2.rearrange("(k p) n -> p k n", p=P)).then_inc(weights_in, 16)
            sp.dma_start(w3_sb[:, :], w3).then_inc(weights_in, 16)
            sp.dma_start(b1_sb[:, :], b1).then_inc(weights_in, 16)
            sp.dma_start(b2_sb[:, :], b2).then_inc(weights_in, 16)
            sp.wait_ge(one_hot_made, 1)
            load_ids_across(2)
            during(1, 1)
            with sp.Fori(1, TILES // 2 - 1) as u:
                for par in range(2):
                    during(u * 2 + par, par)
            for t in range(TILES - 2, TILES):
                during(t, t % 2)
            for t in range(TILES - 2, TILES):
                store_y(t)
            sp.wait_ge(y_out, 16 * TILES)

        @block.gpsimd
        def _(pool):
            def gather(u, par, f0, first):
                t = u * 2 + par
                pool.wait_ge(row_ids_in[par], (u + 1) * 16)
                pool.sem_inc(slots_open, 1)
                for f in range(f0, FIELDS):
                    k = f // TURNED
                    if not first and (f == f0 or f % TURNED == 0):
                        pool.wait_ge(step_turned, (t - 1) * STEPS + k + 1)
                        pool.sem_inc(slots_open, 1)
                    pool.indirect_dma_start(
                        out=rows[:, f, :], out_offset=None, in_=tables[f],
                        in_offset=bass.IndirectOffsetOnAxis(ap=row_ids[par][:, f:f + 1], axis=0),
                    ).then_inc(gathered[k], 16)

            pool.memset(ident[:, :], 0.0).then_inc(ident_zero, 1)
            pool.wait_ge(ident_zero, 1)
            pool.affine_select(out=ident[:, :], in_=ident[:, :], compare_op=ALU.not_equal, fill=1.0,
                               base=0, pattern=[[-1, P]], channel_multiplier=1).then_inc(ident_ready, 1)
            pool.iota(sub_row[:, :], pattern=[[1, SUB]], base=0, channel_multiplier=SUB).then_inc(sub_row_ready, 1)
            gather(0, 0, 0, True)
            gather(0, 1, SMALL, False)
            with pool.Fori(1, TILES // 2) as u:
                for par in range(2):
                    gather(u, par, SMALL, False)

        @block.tensor
        def _(pe):
            def turn(t, k):
                if k == 0:
                    pe.wait_ge(gathered[0], 16 * TURNED + t * 16 * GATHERED0)
                    if not (isinstance(t, int) and t == 0):
                        pe.wait_ge(produced_kept, t * SMALL)
                else:
                    pe.wait_ge(gathered[k], (t + 1) * 16 * TURNED)
                if k in (4, 5):
                    if not (isinstance(t, int) and t == TILES - 1):
                        pe.wait_ge(produced_kept, t * SMALL + k - 3)
                elif not (isinstance(t, int) and t == 0 and k < 2):
                    pe.wait_ge(act_kept, t * STEPS + k - 1)
                    pe.wait_ge(dve_kept, t * STEPS + k - 1)
                if isinstance(t, int) and t == TILES - 1 and k in (4, 5):
                    pe.wait_ge(act_kept, t * STEPS + k - 1)
                    pe.wait_ge(dve_kept, t * STEPS + k - 1)
                for c in range(CHUNKS):
                    for j in range(TURNED):
                        last = pe.transpose(work_ps[k % 2][:, c, j * P:(j + 1) * P],
                                            rows[:, k * TURNED + j, c * P:(c + 1) * P], ident[:, :])
                last.then_inc(step_turned, 1)

            def produce(t, f):
                if f == 0:
                    pe.wait_ge(one_hot_made, t)
                    if isinstance(t, int) and t == 1:
                        pe.wait_ge(low_ready, SMALL)
                pe.wait_ge(act_kept, (t - 1) * STEPS + f + 3)
                pe.wait_ge(dve_kept, (t - 1) * STEPS + f + 3)
                for r in range(SUB):
                    last = pe.matmul(work_ps[f][:, 0, :], one_hot[:, r, f, :],
                                     small[:, f, r, :, :].rearrange("p a d -> p (a d)"),
                                     start=(r == 0), stop=(r == SUB - 1))
                last.then_inc(produced, 1)

            def gram(t, par, portion):
                if portion == 0:
                    pe.wait_ge(act_kept, (t + 1) * STEPS)
                    pe.wait_ge(dve_kept, (t + 1) * STEPS)
                if not (isinstance(t, int) and t == 0 and portion < 2):
                    pe.wait_ge(dve_cut if portion % 2 else act_cut, t * (PORTIONS // 2) + portion // 2)
                for g in range(GPP):
                    for c in range(CHUNKS):
                        four = quads[par][:, c, portion * GPP + g, :]
                        last = pe.matmul(gram_ps[portion % 2][:, g, :], four, four,
                                         start=(c == 0), stop=(c == CHUNKS - 1))
                last.then_inc(gram_done, 1)

            def turn_features(t):
                pe.wait_ge(picked, (t + 1) * 2)
                pe.wait_ge(dense_in, (t + 1) * 16)
                if not (isinstance(t, int) and t == 0):
                    pe.wait_ge(y_kept, t)
                for c in range(KC):
                    last = pe.transpose(bank_a[:, c * P:(c + 1) * P],
                                        features[:, c * P:(c + 1) * P], ident[:, :])
                last.then_inc(ft_done, 1)

            def layer1(t):
                pe.wait_ge(ft_kept, t + 1)
                for m in range(M1):
                    for c in range(KC):
                        last = pe.matmul(bank_b[:, m * P:(m + 1) * P], w1_sb[:, c, m * P:(m + 1) * P],
                                         features_t[:, c, :], start=(c == 0), stop=(c == KC - 1))
                last.then_inc(h1_done, 1)

            def layer2(t):
                pe.wait_ge(h1_kept, (t + 1) * M1)
                for m in range(M2):
                    for c in range(M1):
                        last = pe.matmul(bank_a[:, m * P:(m + 1) * P], w2_sb[:, c, m * P:(m + 1) * P],
                                         hidden1[:, c, :], start=(c == 0), stop=(c == M1 - 1))
                last.then_inc(h2_done, 1)

            def layer3(t):
                pe.wait_ge(h2_kept, (t + 1) * M2)
                for c in range(M2):
                    last = pe.matmul(bank_a[0:1, M2 * P:(M2 + 1) * P], w3_sb[:, c:c + 1],
                                     hidden2[:, c, :], start=(c == 0), stop=(c == M2 - 1))
                last.then_inc(y_done, 1)

            def tile(t, par, before, produces):
                for k in range(STEPS):
                    turn(t, k)
                    if before and k < 4:
                        gram(t - 1, 1 - par, 2 * k)
                        gram(t - 1, 1 - par, 2 * k + 1)
                    if produces and k == 3:
                        for f in range(SMALL):
                            produce(t + 1, f)
                    if before and k == 4:
                        turn_features(t - 1)
                    if before and k == 5:
                        layer1(t - 1)
                    if before and k == 6:
                        layer2(t - 1)
                    if before and k == 7:
                        layer3(t - 1)

            pe.wait_ge(ident_ready, 1)
            tile(0, 0, False, True)
            pe.wait_ge(weights_in, 16 * LOADED)
            tile(1, 1, True, True)
            with pe.Fori(1, TILES // 2 - 1) as u:
                for par in range(2):
                    tile(u * 2 + par, par, True, True)
            tile(TILES - 2, 0, True, True)
            tile(TILES - 1, 1, True, False)
            for portion in range(PORTIONS):
                gram(TILES - 1, 1, portion)
            turn_features(TILES - 1)
            layer1(TILES - 1)
            layer2(TILES - 1)
            layer3(TILES - 1)

        @block.scalar
        def _(act):
            def keep_turned(t, par, k):
                act.wait_ge(step_turned, t * STEPS + k + 1)
                if k == 0 and not (isinstance(t, int) and t < 2):
                    act.wait_ge(gram_done, (t - 1) * PORTIONS)
                act.activation(kept[par][:, 0, :, :, k * TURNED:(k + 1) * TURNED],
                               work_ps[k % 2][:, 0, :].rearrange("p (f q g) -> p q g f", f=TURNED, q=QUADS),
                               ACT.Copy).then_inc(act_kept, 1)

            def cut_even(t, portion):
                act.wait_ge(gram_done, t * PORTIONS + portion + 1)
                if portion == 0 and not (isinstance(t, int) and t == 0):
                    act.wait_ge(unfolded, t)
                cut(lambda dst, src: act.activation(dst, src, ACT.Copy), portion).then_inc(act_cut, 1)

            def pick(t):
                act.wait_ge(unfolded, t + 1)
                act.activation(square[:, :, FIELDS:ZROW], square[:, :, 0:HALF], ACT.Copy).then_inc(wrapped, 1)
                act.wait_ge(wrapped, t + 1)
                if not (isinstance(t, int) and t == 0):
                    act.wait_ge(ft_done, t)
                act.activation(features[:, 0:CYCLIC].rearrange("p (i k) -> p i k", i=FIELDS),
                               diagonal[:, :, 1:HALF], ACT.Copy).then_inc(picked, 1)
                act.activation(features[:, CYCLIC:PAIRS], diagonal[:, 0:HALF, HALF],
                               ACT.Copy).then_inc(picked, 1)

            def keep_features(t):
                act.wait_ge(ft_done, t + 1)
                act.activation(features_t[:, :, :], bank_a[:, :].rearrange("p (k s) -> p k s", k=KC),
                               ACT.Copy).then_inc(ft_kept, 1)

            def keep_hidden1(t):
                act.wait_ge(h1_done, t + 1)
                for m in range(M1):
                    act.activation(hidden1[:, m, :], bank_b[:, m * P:(m + 1) * P], ACT.Relu,
                                   bias=b1_sb[:, m:m + 1]).then_inc(h1_kept, 1)

            def keep_hidden2(t):
                act.wait_ge(h2_done, t + 1)
                for m in range(M2):
                    act.activation(hidden2[:, m, :], bank_a[:, m * P:(m + 1) * P], ACT.Relu,
                                   bias=b2_sb[:, m:m + 1]).then_inc(h2_kept, 1)

            def keep_y(t):
                act.wait_ge(y_done, t + 1)
                if not (isinstance(t, int) and t == 0):
                    act.wait_ge(y_out, t * 16)
                act.activation(y_sb[:, :], bank_a[0:1, M2 * P:(M2 + 1) * P], ACT.Copy).then_inc(y_kept, 1)

            def tile(t, par, before):
                for k in range(STEPS):
                    keep_turned(t, par, k)
                    if before and k < 4:
                        cut_even(t - 1, 2 * k)
                    if before and k == 3:
                        pick(t - 1)
                    if before and k == 4:
                        keep_features(t - 1)
                    if before and k == 5:
                        keep_hidden1(t - 1)
                    if before and k == 6:
                        keep_hidden2(t - 1)
                    if before and k == 7:
                        keep_y(t - 1)

            act.wait_ge(small_in, 16 * SMALL)
            for i in range(SMALL):
                act.activation(small[:, i, :, 0, :], small_raw[:, i, :, :], ACT.Copy).then_inc(high_ready, 1)
            tile(0, 0, False)
            act.wait_ge(low_ready, SMALL)
            act.wait_ge(weights_in, 16 * LOADED)
            tile(1, 1, True)
            with act.Fori(1, TILES // 2 - 1) as u:
                for par in range(2):
                    tile(u * 2 + par, par, True)
            tile(TILES - 2, 0, True)
            tile(TILES - 1, 1, True)
            for portion in range(0, PORTIONS, 2):
                cut_even(TILES - 1, portion)
            pick(TILES - 1)
            keep_features(TILES - 1)
            keep_hidden1(TILES - 1)
            keep_hidden2(TILES - 1)
            keep_y(TILES - 1)

        @block.vector
        def _(dve):
            def keep_turned(t, par, k):
                dve.wait_ge(step_turned, t * STEPS + k + 1)
                if k == 0 and not (isinstance(t, int) and t < 2):
                    dve.wait_ge(gram_done, (t - 1) * PORTIONS)
                dve.tensor_copy(kept[par][:, 1, :, :, k * TURNED:(k + 1) * TURNED],
                                work_ps[k % 2][:, 1, :].rearrange("p (f q g) -> p q g f", f=TURNED, q=QUADS),
                                ).then_inc(dve_kept, 1)

            def cut_odd(t, portion):
                dve.wait_ge(gram_done, t * PORTIONS + portion + 1)
                if portion == 1 and not (isinstance(t, int) and t == 0):
                    dve.wait_ge(unfolded, t)
                cut(dve.tensor_copy, portion).then_inc(dve_cut, 1)

            def unfold(t):
                dve.wait_ge(act_cut, (t + 1) * (PORTIONS // 2))
                dve.wait_ge(dve_cut, (t + 1) * (PORTIONS // 2))
                if not (isinstance(t, int) and t == 0):
                    dve.wait_ge(picked, t * 2)
                dve.transpose(square[:, :, 0:FIELDS],
                              gram_sb[:, :, :].rearrange("p g j -> p j g")).then_inc(unfolded, 1)

            def keep_produced(t, f):
                dve.wait_ge(produced, (t - 1) * SMALL + f + 1)
                dve.reduce_sum(rows[:, f, :], work_ps[f][:, 0, :].rearrange("p (a d) -> p d a", a=2),
                               axis=mybir.AxisListType.X).then_inc(produced_kept, 1)

            def make_one_hot(t, part):
                if part == 0:
                    dve.wait_ge(ids_across_in, t * 16)
                    if not (isinstance(t, int) and t == 1):
                        dve.wait_ge(produced, (t - 1) * SMALL)
                quarter = SUB // 4
                for r in range(part * quarter, (part + 1) * quarter):
                    last = dve.tensor_tensor(one_hot[:, r, :, :].rearrange("p f s -> p (f s)"),
                                             ids_across[:, :, :].rearrange("p f s -> p (f s)"),
                                             sub_row[:, r:r + 1].to_broadcast([SP, SMALL * P]), ALU.is_equal)
                if part == 3:
                    last.then_inc(one_hot_made, 1)

            def tile(t, par, before, produces, makes):
                for k in range(STEPS):
                    keep_turned(t, par, k)
                    if before and k < 4:
                        cut_odd(t - 1, 2 * k + 1)
                    if before and k == 3:
                        unfold(t - 1)
                    if produces and k == 3:
                        for f in range(SMALL):
                            keep_produced(t + 1, f)
                    if makes and k >= 4:
                        make_one_hot(t + 2, k - 4)

            dve.wait_ge(sub_row_ready, 1)
            for part in range(4):
                make_one_hot(1, part)
            for i in range(SMALL):
                dve.wait_ge(high_ready, i + 1)
                dve.tensor_tensor(small[:, i, :, 1, :], small_raw[:, i, :, :], small[:, i, :, 0, :],
                                  ALU.subtract).then_inc(low_ready, 1)
            tile(0, 0, False, True, True)
            dve.wait_ge(low_ready, SMALL)
            tile(1, 1, True, True, True)
            with dve.Fori(1, TILES // 2 - 1) as u:
                for par in range(2):
                    tile(u * 2 + par, par, True, True, True)
            tile(TILES - 2, 0, True, True, False)
            tile(TILES - 1, 1, True, False, False)
            for portion in range(1, PORTIONS, 2):
                cut_odd(TILES - 1, portion)
            unfold(TILES - 1)


def kernel(**inputs):
    import concourse.bacc as bacc
    from concourse.bass_utils import run_bass_kernel_spmd

    nc = bacc.Bacc("TRN2", target_bir_lowering=False, num_devices=1)
    laid = {name: np.ascontiguousarray(a) for name, a in inputs.items()}
    laid["W_top1"] = np.ascontiguousarray(laid["W_top1"][pair_order()])
    laid["ids"] = np.ascontiguousarray(laid["ids"][:, SLOTS])
    laid["small_ids"] = np.ascontiguousarray(laid["ids"][:, :SMALL].T)
    for name in ("b_top1", "b_top2", "W_top3"):
        laid[name] = np.ascontiguousarray(laid[name].reshape(-1, P).T)
    arrays, aps = {}, {}
    for name, a in laid.items():
        arrays[f"in_{name}"] = a
        aps[name] = nc.dram_tensor(f"in_{name}", a.shape, mybir.dt.from_np(a.dtype), kind="ExternalInput").ap()
    out = nc.dram_tensor("out_y", (1, BATCH), mybir.dt.float32, kind="ExternalOutput").ap()
    dlrm_tower(nc, aps["dense_ctx"], aps["ids"], aps["small_ids"], [aps[f"tbl_{f}"] for f in SLOTS],
               aps["W_top1"], aps["b_top1"], aps["W_top2"], aps["b_top2"], aps["W_top3"], out)
    r = run_bass_kernel_spmd(nc, [arrays], core_ids=[0])
    return r.results[0]["out_y"].reshape(BATCH, 1)
```

```python
from contextlib import ExitStack

import numpy as np

import concourse.bass as bass
import concourse.mybir as mybir

FIELDS = 32
D = 256
P = 128
BATCH = 2048
CONTEXT = 16
HALF = FIELDS // 2
PAIRS = FIELDS * (FIELDS - 1) // 2
CYCLIC = FIELDS * (HALF - 1)
HIDDEN1 = 512
HIDDEN2 = 256
SMALL_ROWS = 1000
SMALL_FIELDS = [2, 4, 5, 6]
SMALL = len(SMALL_FIELDS)
SLOTS = SMALL_FIELDS + [f for f in range(FIELDS) if f not in SMALL_FIELDS]


def pair_order():
    upper = np.zeros((FIELDS, FIELDS), np.int64)
    rows, cols = np.triu_indices(FIELDS, k=1)
    upper[rows, cols] = upper[cols, rows] = np.arange(PAIRS)
    upper = upper[np.ix_(SLOTS, SLOTS)]
    order = [upper[i, (i + k) % FIELDS] for i in range(FIELDS) for k in range(1, HALF)]
    order += [upper[i, i + HALF] for i in range(HALF)]
    order += list(range(PAIRS, PAIRS + CONTEXT))
    return np.array(order)


def dlrm_tower(nc, dense_ctx, ids, small_ids, tables, w1, b1, w2, b2, w3, out):
    fp32 = mybir.dt.float32
    fp32r = mybir.dt.float32r
    int32 = mybir.dt.int32
    ALU = mybir.AluOpType
    ACT = mybir.ActivationFunctionType

    TILES = BATCH // P
    CHUNKS = D // P
    TURNED = 4
    STEPS = FIELDS // TURNED
    LAST_DVE = 4
    BLOCK = 32
    DB = P // BLOCK
    QUADS = P // FIELDS
    GROUPS = P // QUADS
    PORTIONS = 8
    GPP = GROUPS // PORTIONS
    FEATURES = PAIRS + CONTEXT
    COLS = FIELDS - 1
    KC = FEATURES // P
    M1 = HIDDEN1 // P
    ZROW = FIELDS + HALF
    SUB = 8
    SP = SMALL_ROWS // SUB
    ACT_SUB = 3
    AT_ONCE = SMALL // 2
    SMALL_ORDER = [2, 3, 0, 1]
    PICKS = 3
    LOADED = KC + 4

    ctx = ExitStack()
    with ctx:
        def sbuf(name, shape, dt=fp32):
            return ctx.enter_context(nc.sbuf_tensor(name, shape, dt))

        def psum(name, shape):
            return ctx.enter_context(nc.psum_tensor(name, shape, fp32))

        def sem(name):
            return ctx.enter_context(nc.semaphore(name))

        row_ids = [sbuf(f"row_ids{i}", [P, FIELDS], int32) for i in range(2)]
        ids_across = sbuf("ids_across", [SP, AT_ONCE, 2 * P], int32)
        sub_row = sbuf("sub_row", [SP, SUB], int32)
        sub_row_f = sbuf("sub_row_f", [SP, SUB])
        one_hot = sbuf("one_hot", [SP, SUB, AT_ONCE, 2 * P], fp32r)
        small = sbuf("small", [SP, SMALL, SUB, 2, D], fp32r)
        rows = sbuf("rows", [P, FIELDS - SMALL, D])
        turned = [sbuf(f"turned{i}", [P, CHUNKS, P, FIELDS]) for i in range(2)]
        ahead = sbuf("ahead", [P, CHUNKS, P, AT_ONCE])
        gram_sb = sbuf("gram_sb", [P, GROUPS, COLS])
        products = sbuf("products", [P, COLS * (ZROW + 1)])
        features = sbuf("features", [P, FEATURES])
        features_t = sbuf("features_t", [P, KC, P])
        hidden1 = sbuf("hidden1", [P, M1, P])
        hidden2 = sbuf("hidden2", [P, HIDDEN2])
        y_sb = [sbuf(f"y_sb{i}", [P, 1]) for i in range(2)]
        w1_sb = sbuf("w1_sb", [P, KC, HIDDEN1])
        w2_sb = sbuf("w2_sb", [P, M1, HIDDEN2])
        w3_sb = sbuf("w3_sb", [P, HIDDEN2])
        b1_sb = sbuf("b1_sb", [P, M1])
        b2_sb = sbuf("b2_sb", [P, HIDDEN2])
        ident = sbuf("ident", [P, P])

        work_ps = [psum(f"work_ps{i}", [P, 2, 512]) for i in range(2)]
        gram_banks = [psum(f"gram_ps{i}", [P, GPP * P]) for i in range(2)]
        bank_a = psum("bank_a", [P, KC * P])
        bank_b = psum("bank_b", [P, M1 * P])

        row_ids_in = [sem(f"row_ids_in{i}") for i in range(2)]
        ids_across_in = sem("ids_across_in")
        dense_in = sem("dense_in")
        weights_in = sem("weights_in")
        small_in = [sem(f"small_in{i}") for i in range(SMALL)]
        small_gathered = sem("small_gathered")
        gathered = {k: sem(f"gathered{k}") for k in range(1, STEPS)}
        ids_spent = sem("ids_spent")
        slots_open = sem("slots_open")
        ident_zero = sem("ident_zero")
        ident_ready = sem("ident_ready")
        sub_row_ready = sem("sub_row_ready")
        sub_row_f_ready = sem("sub_row_f_ready")
        high_ready = sem("high_ready")
        low_ready = sem("low_ready")
        one_hot_made = sem("one_hot_made")
        distances = sem("distances")
        one_hot_act = sem("one_hot_act")
        produced = sem("produced")
        produced_kept = sem("produced_kept")
        ahead_placed = sem("ahead_placed")
        dve_turned = sem("dve_turned")
        step_turned = sem("step_turned")
        act_kept = sem("act_kept")
        gram_done = sem("gram_done")
        cut_out = sem("cut_out")
        unfolded = sem("unfolded")
        wrapped = sem("wrapped")
        picked = sem("picked")
        ft_done = sem("ft_done")
        ft_kept = sem("ft_kept")
        h1_done = sem("h1_done")
        h1_kept = sem("h1_kept")
        h2_done = sem("h2_done")
        h2_kept = sem("h2_kept")
        y_done = sem("y_done")
        y_out = [sem(f"y_out{i}") for i in range(2)]

        gram_ps = [b[:, 0:GPP * QUADS * COLS].rearrange("p (g q j) -> p g q j", g=GPP, q=QUADS) for b in gram_banks]

        block = ctx.enter_context(nc.Block())

        small_raw = turned[1][0:SP, :, :, :].rearrange("p c s f -> p (c s f)").rearrange(
            "p (t r d) -> p t r d", t=SMALL, r=SUB)
        small_rows = products[:, 0:AT_ONCE * D].rearrange("p (f d) -> p f d", f=AT_ONCE)
        square = products[:, 0:COLS * ZROW].rearrange("p (i j) -> p i j", j=ZROW)
        diagonal = products[:, :].rearrange("p (i k) -> p i k", k=ZROW + 1)
        quads = [t[:, :, :, :].rearrange("d c (g q) f -> d c g (q f)", q=QUADS) for t in turned]
        columns = [t[:, :, :, 0:COLS].rearrange("d c (g q) f -> d c g q f", q=QUADS) for t in turned]
        blocks = [t[:, :, :, :].rearrange("d c (g q) f -> d f c q g", q=QUADS) for t in turned]
        kept = [t[:, :, :, :].rearrange("d c (g q) f -> d c q g f", q=QUADS) for t in turned]

        ahead_kept = ahead[:, :, :, :].rearrange("d c (g q) f -> d c q g f", q=QUADS)

        def looked_up(parity_n):
            return AT_ONCE * (1 - parity_n)

        def last_dve(t):
            if isinstance(t, int) and t == 0:
                return 2
            if isinstance(t, int) and t == TILES - 1:
                return 2
            return LAST_DVE

        def by_dve(t, k):
            if isinstance(t, int) and t == 0:
                return 1 + k
            return by_dve(0, last_dve(0)) + (t - 1) * LAST_DVE + k

        def by_pe(t, k):
            if isinstance(t, int) and t == 0:
                return k - last_dve(0)
            return by_pe(0, STEPS - 1) + (t - 1) * (STEPS - 1 - LAST_DVE) + k - last_dve(t)

        def hidden1_banks(t):
            return [bank_b, work_ps[0][:, 0, :] if isinstance(t, int) and t == TILES - 1 else bank_b]

        def pair_of(t, k):
            if isinstance(t, int) and t == 0:
                return {3: 0, 4: 0, 5: 1, 6: 0, 7: 1}[k]
            if isinstance(t, int) and t == TILES - 1:
                return 1 - k % 2
            return {5: 0, 6: 0, 7: 1}[k]

        @block.sync
        def _(sp):
            def load_row_ids(t, par):
                sp.dma_start(row_ids[par][:, :], ids[bass.ds(t * P, P), :]).then_inc(row_ids_in[par], 16)

            def load_ids_across(n, parity):
                at = looked_up(parity)
                sp.dma_start(ids_across[:, :, :],
                             small_ids[at:at + AT_ONCE, bass.ds(n * P, 2 * P)].partition_broadcast(SP),
                             ).then_inc(ids_across_in, 16)

            def load_dense(t):
                sp.dma_start(features[:, PAIRS:FEATURES],
                             dense_ctx[bass.ds(t * P, P), :]).then_inc(dense_in, 16)

            def store_y(t, par):
                sp.wait_ge(y_done, t + 1)
                sp.dma_start(out[bass.ds(t * P, P), :], y_sb[par][:, :]).then_inc(y_out[par], 16)

            def during(t, par):
                if not (isinstance(t, int) and t == TILES - 1):
                    sp.wait_ge(dve_turned, by_dve(t - 1, last_dve(t - 1)))
                    sp.sem_inc(ids_spent, 1)
                    sp.wait_ge(step_turned, by_pe(t - 1, STEPS - 1))
                    load_row_ids(t + 1, 1 - par)
                if not (isinstance(t, int) and t >= TILES - 2):
                    sp.wait_ge(one_hot_made, t + 2)
                    sp.sem_inc(ids_spent, 1)
                    sp.wait_ge(distances, (t + 1) * ACT_SUB)
                    load_ids_across(t + 2, par)
                if not (isinstance(t, int) and t < 2):
                    store_y(t - 2, par)
                sp.wait_ge(ft_done, t)
                load_dense(t)

            load_row_ids(0, 0)
            load_ids_across(0, 0)
            for i in range(2):
                sp.sem_inc(y_out[i], 16)
            for i in SMALL_ORDER:
                sp.dma_start(small_raw[:, i, :, :], tables[i].rearrange("(p r) d -> p r d", r=SUB),
                             ).then_inc(small_in[i], 16)
            load_row_ids(1, 1)
            load_dense(0)
            for n in (1, 2):
                sp.wait_ge(one_hot_made, n)
                if n == 2:
                    sp.wait_ge(distances, ACT_SUB)
                load_ids_across(n, n % 2)
            def after_step(k):
                sp.wait_ge(gathered[k], 2 * 16 * TURNED)

            for c in range(KC):
                after_step(1 + c)
                sp.dma_start(w1_sb[:, c, :], w1[c * P:(c + 1) * P, :]).then_inc(weights_in, 16)
            after_step(5)
            sp.dma_start(w2_sb[:, :, :], w2.rearrange("(k p) n -> p k n", p=P)).then_inc(weights_in, 16)
            sp.dma_start(w3_sb[:, :], w3.rearrange("n a -> (a n)").partition_broadcast(P)).then_inc(weights_in, 16)
            sp.dma_start(b1_sb[:, :], b1).then_inc(weights_in, 16)
            sp.dma_start(b2_sb[:, :], b2.partition_broadcast(P)).then_inc(weights_in, 16)
            during(1, 1)
            with sp.Fori(1, TILES // 2 - 1) as u:
                for par in range(2):
                    during(u * 2 + par, par)
            for t in range(TILES - 2, TILES):
                during(t, t % 2)
            for t in range(TILES - 2, TILES):
                store_y(t, t % 2)
            for i in range(2):
                sp.wait_ge(y_out[i], 16 * (TILES // 2 + 1))

        @block.gpsimd
        def _(pool):
            def fetch(table, par, into, done):
                pool.indirect_dma_start(
                    out=into, out_offset=None, in_=tables[table],
                    in_offset=bass.IndirectOffsetOnAxis(ap=row_ids[par][:, table:table + 1], axis=0),
                ).then_inc(done, 16)

            def gather(u, par, first):
                t = u * 2 + par
                pool.wait_ge(row_ids_in[par], (u + 1) * 16)
                pool.sem_inc(slots_open, 1)
                if first:
                    for f in range(AT_ONCE):
                        fetch(f, par, small_rows[:, f, :], small_gathered)
                for k in range(1, STEPS):
                    if not first:
                        if k <= last_dve(t - 1):
                            pool.wait_ge(dve_turned, by_dve(t - 1, k))
                        else:
                            pool.wait_ge(step_turned, by_pe(t - 1, k))
                        pool.sem_inc(slots_open, 1)
                    for f in range(k * TURNED, (k + 1) * TURNED):
                        fetch(f, par, rows[:, f - SMALL, :], gathered[k])

            pool.memset(ident[:, :], 0.0).then_inc(ident_zero, 1)
            pool.wait_ge(ident_zero, 1)
            pool.affine_select(out=ident[:, :], in_=ident[:, :], compare_op=ALU.not_equal, fill=1.0,
                               base=0, pattern=[[-1, P]], channel_multiplier=1).then_inc(ident_ready, 1)
            pool.iota(sub_row[:, :], pattern=[[1, SUB]], base=0, channel_multiplier=SUB).then_inc(sub_row_ready, 1)
            gather(0, 0, True)
            gather(0, 1, False)
            with pool.Fori(1, TILES // 2) as u:
                for par in range(2):
                    gather(u, par, False)

        @block.tensor
        def _(pe):
            def turn(t, k):
                pe.wait_ge(gathered[k], (t + 1) * 16 * TURNED)
                if isinstance(t, int) and t == 0:
                    if k == 5:
                        pe.wait_ge(produced_kept, 2 * AT_ONCE)
                    elif k > 3:
                        pe.wait_ge(act_kept, by_pe(0, {4: 3, 6: 4, 7: 5}[k]))
                elif isinstance(t, int) and t == TILES - 1:
                    pe.wait_ge(act_kept, by_pe(t - 1, k + 3) if k < 5 else by_pe(t, k - 2))
                elif k == 5:
                    pe.wait_ge(act_kept, by_pe(t - 1, 6))
                elif k == 6:
                    pe.wait_ge(act_kept, by_pe(t, 5))
                else:
                    pe.wait_ge(produced_kept, (t + 2) * AT_ONCE)
                for c in range(CHUNKS):
                    for j in range(TURNED):
                        last = pe.transpose(work_ps[pair_of(t, k)][:, c, j * P:(j + 1) * P],
                                            rows[:, k * TURNED + j - SMALL, c * P:(c + 1) * P], ident[:, :])
                last.then_inc(step_turned, 1)

            def look_up(n, parity):
                pe.wait_ge(one_hot_made, n + 1)
                if not (isinstance(n, int) and n == 0):
                    pe.wait_ge(one_hot_act, n)
                if isinstance(n, int) and n == 1:
                    pe.wait_ge(produced_kept, AT_ONCE)
                elif not (isinstance(n, int) and n == 0):
                    pe.wait_ge(act_kept, by_pe(n - 2, STEPS - 1))
                for f in range(AT_ONCE):
                    if isinstance(n, int) and n <= 1:
                        pe.wait_ge(low_ready, n * AT_ONCE + f + 1)
                    for c in range(CHUNKS):
                        for r in range(SUB):
                            for part in range(2):
                                last = pe.matmul(work_ps[1][:, f, c * 2 * P:(c + 1) * 2 * P],
                                                 small[:, looked_up(parity) + f, r, part, c * P:(c + 1) * P],
                                                 one_hot[:, r, f, :], start=(r == 0 and part == 0),
                                                 stop=(r == SUB - 1 and part == 1))
                    last.then_inc(produced, 1)

            def gram(t, par, portion):
                if portion == 0:
                    pe.wait_ge(act_kept, by_pe(t, STEPS - 1))
                    pe.wait_ge(dve_turned, by_dve(t, last_dve(t)))
                if not (isinstance(t, int) and t == 0 and portion < 2):
                    pe.wait_ge(cut_out, t * PORTIONS + portion - 1)
                for g in range(GPP):
                    for c in range(CHUNKS):
                        group = portion * GPP + g
                        last = pe.matmul(gram_ps[portion % 2][:, g, :, :], quads[par][:, c, group, :],
                                         columns[par][:, c, group, :, :],
                                         start=(c == 0), stop=(c == CHUNKS - 1))
                last.then_inc(gram_done, 1)

            def turn_features(t):
                pe.wait_ge(picked, t * PICKS + 1)
                if not (isinstance(t, int) and t == 0):
                    pe.wait_ge(h2_kept, t)
                for c in range(KC):
                    if c == KC - 1:
                        pe.wait_ge(picked, (t + 1) * PICKS)
                        pe.wait_ge(dense_in, (t + 1) * 16)
                    last = pe.transpose(bank_a[:, c * P:(c + 1) * P],
                                        features[:, c * P:(c + 1) * P], ident[:, :])
                last.then_inc(ft_done, 1)

            def layer1(t):
                halves = hidden1_banks(t)
                pe.wait_ge(ft_kept, t + 1)
                if isinstance(t, int) and t == 0:
                    pe.wait_ge(weights_in, 16 * LOADED)
                for m in range(M1):
                    for c in range(KC):
                        last = pe.matmul(halves[m // 2][:, m * P:(m + 1) * P], w1_sb[:, c, m * P:(m + 1) * P],
                                         features_t[:, c, :], start=(c == 0), stop=(c == KC - 1))
                    if m % 2 == 1:
                        last.then_inc(h1_done, 1)

            def layer2(t):
                for c in range(M1):
                    pe.wait_ge(h1_kept, t * M1 + c + 1)
                    last = pe.matmul(bank_a[:, 0:HIDDEN2], hidden1[:, c, :], w2_sb[:, c, :],
                                     start=(c == 0), stop=(c == M1 - 1))
                last.then_inc(h2_done, 1)

            def tile(t, par):
                for portion in range(PORTIONS):
                    gram(t - 1, 1 - par, portion)
                look_up(t + 1, 1 - par)
                turn_features(t - 1)
                turn(t, 5)
                layer1(t - 1)
                turn(t, 6)
                turn(t, 7)
                if not (isinstance(t, int) and t == TILES - 2):
                    layer2(t - 1)

            look_up(0, 0)
            pe.wait_ge(ident_ready, 1)
            turn(0, 3)
            look_up(1, 1)
            for k in range(4, STEPS):
                turn(0, k)
            tile(1, 1)
            with pe.Fori(1, TILES // 2 - 1) as u:
                for par in range(2):
                    tile(u * 2 + par, par)
            tile(TILES - 2, 0)
            for portion in range(PORTIONS):
                gram(TILES - 2, 0, portion)
            turn(TILES - 1, 3)
            turn(TILES - 1, 4)
            layer2(TILES - 3)
            turn_features(TILES - 2)
            turn(TILES - 1, 5)
            turn(TILES - 1, 6)
            layer1(TILES - 2)
            turn(TILES - 1, 7)
            for portion in range(PORTIONS):
                gram(TILES - 1, 1, portion)
            layer2(TILES - 2)
            turn_features(TILES - 1)
            layer1(TILES - 1)
            layer2(TILES - 1)

        @block.scalar
        def _(act):
            def keep_turned(t, par, k):
                act.wait_ge(step_turned, by_pe(t, k))
                for c in range(CHUNKS):
                    last = act.activation(
                        kept[par][:, c, :, :, k * TURNED:(k + 1) * TURNED],
                        work_ps[pair_of(t, k)][:, c, :].rearrange("p (f q g) -> p q g f", f=TURNED, q=QUADS), ACT.Copy)
                last.then_inc(act_kept, 1)

            def place_ahead(n, parity):
                act.wait_ge(produced_kept, n * AT_ONCE)
                at = looked_up(1 - parity)
                act.activation(turned[parity][:, :, :, at:at + AT_ONCE], ahead[:, :, :, :],
                               ACT.Copy).then_inc(ahead_placed, 1)

            def keep_produced(n, parity):
                for f in range(AT_ONCE):
                    act.wait_ge(produced, n * AT_ONCE + f + 1)
                    if not (isinstance(n, int) and n == 0):
                        act.wait_ge(ahead_placed, n)
                    field = work_ps[1][:, f, :].rearrange("p (c t q g) -> p c t q g", c=CHUNKS, t=2, q=QUADS)
                    act.activation(kept[parity][:, :, :, :, looked_up(parity) + f], field[:, :, 0, :, :], ACT.Copy)
                    act.activation(ahead_kept[:, :, :, :, f], field[:, :, 1, :, :],
                                   ACT.Copy).then_inc(produced_kept, 1)

            def measure(n):
                act.wait_ge(ids_across_in, (n + 1) * 16)
                act.wait_ge(produced, n * AT_ONCE)
                for sub in range(ACT_SUB):
                    act.activation(one_hot[:, sub, :, :].rearrange("p f s -> p (f s)"),
                                   ids_across[:, :, :].rearrange("p f s -> p (f s)"), ACT.Abs,
                                   bias=sub_row_f[:, sub:sub + 1], scale=-1.0).then_inc(distances, 1)

            def make_one_hot(n):
                act.wait_ge(distances, n * ACT_SUB)
                part = one_hot[:, 0:ACT_SUB, :, :].rearrange("p r f s -> p (r f s)")
                act.activation(part, part, ACT.Relu, bias=1.0, scale=-1.0).then_inc(one_hot_act, 1)

            def cut(t, portion):
                act.wait_ge(gram_done, t * PORTIONS + portion + 1)
                if portion == 0 and not (isinstance(t, int) and t == 0):
                    act.wait_ge(unfolded, t)
                for q in range(QUADS):
                    at = slice(q * FIELDS, (q + 1) * FIELDS)
                    last = act.activation(gram_sb[at, portion * GPP:(portion + 1) * GPP, :],
                                          gram_ps[portion % 2][at, :, q, :], ACT.Copy)
                last.then_inc(cut_out, 1)

            def pick(t):
                act.wait_ge(unfolded, t + 1)
                act.activation(square[:, FIELDS - HALF + 1:COLS, FIELDS:ZROW],
                               square[:, FIELDS - HALF + 1:COLS, 0:HALF], ACT.Copy).then_inc(wrapped, 1)
                act.wait_ge(wrapped, t + 1)
                if not (isinstance(t, int) and t == 0):
                    act.wait_ge(ft_done, t)
                cyclic = features[:, 0:CYCLIC].rearrange("p (i k) -> p i k", i=FIELDS)
                act.activation(cyclic[:, 0:COLS, :], diagonal[:, 0:COLS, 1:HALF], ACT.Copy).then_inc(picked, 1)
                act.activation(cyclic[:, COLS, :], square[:, 0:HALF - 1, COLS], ACT.Copy).then_inc(picked, 1)
                act.activation(features[:, CYCLIC:PAIRS], diagonal[:, 0:HALF, HALF],
                               ACT.Copy).then_inc(picked, 1)

            def keep_features(t):
                act.wait_ge(ft_done, t + 1)
                act.activation(features_t[:, :, :], bank_a[:, :].rearrange("p (k s) -> p k s", k=KC),
                               ACT.Copy).then_inc(ft_kept, 1)

            def keep_hidden1(t):
                halves = hidden1_banks(t)
                act.wait_ge(h1_done, t * 2 + (1 if halves[0] is not halves[1] else 2))
                if isinstance(t, int) and t == 0:
                    act.wait_ge(weights_in, 16 * LOADED)
                for m in range(M1):
                    if m == 2:
                        act.wait_ge(h1_done, t * 2 + 2)
                    act.activation(hidden1[:, m, :], halves[m // 2][:, m * P:(m + 1) * P], ACT.Relu,
                                   bias=b1_sb[:, m:m + 1]).then_inc(h1_kept, 1)

            def tile(t, par, makes):
                for portion in range(PORTIONS):
                    cut(t - 1, portion)
                place_ahead(t + 1, 1 - par)
                pick(t - 1)
                keep_produced(t + 1, 1 - par)
                keep_features(t - 1)
                keep_turned(t, par, 5)
                if makes:
                    measure(t + 2)
                keep_hidden1(t - 1)
                keep_turned(t, par, 6)
                keep_turned(t, par, 7)
                if makes:
                    make_one_hot(t + 2)

            act.wait_ge(sub_row_ready, 1)
            act.activation(sub_row_f[:, :], sub_row[:, :], ACT.Copy).then_inc(sub_row_f_ready, 1)
            for i in SMALL_ORDER:
                act.wait_ge(small_in[i], 16)
                act.activation(small[:, i, :, 0, :], small_raw[:, i, :, :], ACT.Copy).then_inc(high_ready, 1)
            act.wait_ge(sub_row_f_ready, 1)
            keep_produced(0, 0)
            measure(1)
            make_one_hot(1)
            keep_turned(0, 0, 3)
            act.wait_ge(low_ready, SMALL)
            place_ahead(1, 1)
            keep_produced(1, 1)
            for k in range(4, STEPS):
                keep_turned(0, 0, k)
            measure(2)
            make_one_hot(2)
            tile(1, 1, True)
            with act.Fori(1, TILES // 2 - 1) as u:
                for par in range(2):
                    tile(u * 2 + par, par, True)
            tile(TILES - 2, 0, False)
            for portion in range(PORTIONS):
                cut(TILES - 2, portion)
            keep_turned(TILES - 1, 1, 3)
            keep_turned(TILES - 1, 1, 4)
            pick(TILES - 2)
            keep_features(TILES - 2)
            for k in range(5, STEPS):
                keep_turned(TILES - 1, 1, k)
            keep_hidden1(TILES - 2)
            for portion in range(PORTIONS):
                cut(TILES - 1, portion)
            pick(TILES - 1)
            keep_features(TILES - 1)
            keep_hidden1(TILES - 1)

        @block.vector
        def _(dve):
            def turn_blocks(par, slots, of_rows):
                for q in range(QUADS):
                    of_quad = of_rows[q * BLOCK:(q + 1) * BLOCK, :, :].rearrange(
                        "s f (c r d) -> s f c r d", c=CHUNKS, r=DB)
                    for r in range(DB):
                        last = dve.transpose(blocks[par][r * BLOCK:(r + 1) * BLOCK, slots, :, q, :],
                                             of_quad[:, :, :, r, :])
                last.then_inc(dve_turned, 1)

            def turn(t, par, k):
                dve.wait_ge(gathered[k], (t + 1) * 16 * TURNED)
                if k == 1 and not (isinstance(t, int) and t < 2):
                    dve.wait_ge(gram_done, (t - 1) * PORTIONS)
                turn_blocks(par, slice(k * TURNED, (k + 1) * TURNED),
                            rows[:, k * TURNED - SMALL:(k + 1) * TURNED - SMALL, :])

            def unfold(t):
                dve.wait_ge(cut_out, (t + 1) * PORTIONS)
                if not (isinstance(t, int) and t == 0):
                    dve.wait_ge(picked, t * PICKS)
                dve.transpose(square[:, 0:COLS, 0:FIELDS],
                              gram_sb[:, :, :].rearrange("p g j -> p j g")).then_inc(unfolded, 1)

            def make_one_hot(n):
                dve.wait_ge(ids_across_in, (n + 1) * 16)
                if not (isinstance(n, int) and n == 0):
                    dve.wait_ge(produced, n * AT_ONCE)
                for sub in range(0 if isinstance(n, int) and n == 0 else ACT_SUB, SUB):
                    last = dve.tensor_tensor(one_hot[:, sub, :, :].rearrange("p f s -> p (f s)"),
                                             ids_across[:, :, :].rearrange("p f s -> p (f s)"),
                                             sub_row[:, sub:sub + 1].to_broadcast([SP, AT_ONCE * 2 * P]),
                                             ALU.is_equal)
                last.then_inc(one_hot_made, 1)

            def last_layers(t, par, before):
                dve.wait_ge(h2_done, t + 1)
                if isinstance(t, int) and t == 0:
                    dve.wait_ge(weights_in, 16 * LOADED)
                if not (isinstance(t, int) and t == 0):
                    dve.wait_ge(y_done, t)
                dve.tensor_tensor(hidden2[:, :], bank_a[:, 0:HIDDEN2], b2_sb[:, :], ALU.add).then_inc(h2_kept, 1)
                dve.wait_ge(h2_kept, t + 1)
                dve.wait_ge(y_out[par], (before + 1) * 16)
                dve.scalar_tensor_tensor(out=hidden2[:, :], in0=hidden2[:, :], scalar=0.0, in1=w3_sb[:, :],
                                         op0=ALU.max, op1=ALU.mult, accum_out=y_sb[par][:, :]).then_inc(y_done, 1)

            def tile(u, par, makes, last_but_one=False):
                t = u * 2 + par
                for k in range(1, LAST_DVE):
                    turn(t, par, k)
                unfold(t - 1)
                turn(t, par, LAST_DVE)
                if makes:
                    make_one_hot(t + 2)
                if not last_but_one:
                    last_layers(t - 1, 1 - par, u - 1 + par)

            def make_low(i, nth):
                dve.wait_ge(high_ready, nth)
                dve.tensor_tensor(small[:, i, :, 1, :], small_raw[:, i, :, :], small[:, i, :, 0, :],
                                  ALU.subtract).then_inc(low_ready, 1)

            dve.wait_ge(sub_row_ready, 1)
            make_one_hot(0)
            for nth, i in enumerate(SMALL_ORDER):
                make_low(i, nth + 1)
            dve.wait_ge(small_gathered, 16 * AT_ONCE)
            turn_blocks(0, slice(0, AT_ONCE), small_rows)
            make_one_hot(1)
            turn(0, 0, 1)
            turn(0, 0, 2)
            make_one_hot(2)
            dve.wait_ge(low_ready, SMALL)
            tile(0, 1, True)
            with dve.Fori(1, TILES // 2 - 1) as u:
                for par in range(2):
                    tile(u, par, True)
            tile(TILES // 2 - 1, 0, False, last_but_one=True)
            turn(TILES - 1, 1, 1)
            turn(TILES - 1, 1, 2)
            unfold(TILES - 2)
            last_layers(TILES - 3, 1, TILES // 2 - 2)
            unfold(TILES - 1)
            last_layers(TILES - 2, 0, TILES // 2 - 1)
            last_layers(TILES - 1, 1, TILES // 2 - 1)


def kernel(**inputs):
    import concourse.bacc as bacc
    from concourse.bass_utils import run_bass_kernel_spmd

    nc = bacc.Bacc("TRN2", target_bir_lowering=False, num_devices=1)
    laid = {name: np.ascontiguousarray(a) for name, a in inputs.items()}
    laid["W_top1"] = np.ascontiguousarray(laid["W_top1"][pair_order()])
    laid["ids"] = np.ascontiguousarray(laid["ids"][:, SLOTS])
    small_ids = laid["ids"][:, :SMALL].T
    laid["small_ids"] = np.ascontiguousarray(np.concatenate([small_ids, small_ids[:, :P]], axis=1))
    laid["b_top1"] = np.ascontiguousarray(laid["b_top1"].reshape(-1, P).T)
    arrays, aps = {}, {}
    for name, a in laid.items():
        arrays[f"in_{name}"] = a
        aps[name] = nc.dram_tensor(f"in_{name}", a.shape, mybir.dt.from_np(a.dtype), kind="ExternalInput").ap()
    out = nc.dram_tensor("out_y", (BATCH, 1), mybir.dt.float32, kind="ExternalOutput").ap()
    dlrm_tower(nc, aps["dense_ctx"], aps["ids"], aps["small_ids"], [aps[f"tbl_{f}"] for f in SLOTS],
               aps["W_top1"], aps["b_top1"], aps["W_top2"], aps["b_top2"], aps["W_top3"], out)
    r = run_bass_kernel_spmd(nc, [arrays], core_ids=[0])
    return r.results[0]["out_y"]
```
